# Optimizing a Trainium2 kernel written in Bass

```python
import numpy as np
import jax
import jax.numpy as jnp

def _softmax(x, axis=-1):
    return jax.nn.softmax(x, axis=axis)

def _gelu(x):
    return jax.nn.gelu(x, approximate=True)

def _silu(x):
    return jax.nn.silu(x)

def _sigmoid(x):
    return jax.nn.sigmoid(x)

def _layernorm(x, axis=-1, eps=1e-05):
    m = jnp.mean(x, axis=axis, keepdims=True)
    v = jnp.var(x, axis=axis, keepdims=True)
    return (x - m) / jnp.sqrt(v + eps)

def _scatter_add(tgt, idx, src, axis=0):
    return tgt.at[idx].add(src)

def _segment_sum(src, seg, n):
    return jax.ops.segment_sum(src, seg, n)
kernel_name = 'mk_decoder_preln_d1_seqx_r8_4a897d'

def setup_inputs(seed: int=0):
    np.random.seed(seed)
    _w = jnp.asarray

    def _rec_inputs():
        import jax
        import jax.numpy as jnp
        _rk = jax.random.key(seed)
        x = -0.0002928 + 1 * jax.random.normal(jax.random.fold_in(_rk, 1), (32, 64, 512), jnp.float32)
        _lenS = 64 - jax.random.randint(jax.random.fold_in(_rk, 7), (32,), 0, max(1, 64 // 4) + 1, jnp.int32)
        _lenS2 = 64 - jax.random.randint(jax.random.fold_in(_rk, 8), (32,), 0, max(1, 64 // 4) + 1, jnp.int32)
        _ctx_4096P = jax.random.normal(jax.random.fold_in(_rk, 11), (32, 16, 512), jnp.float32)
        _ctx_4096c = jax.random.dirichlet(jax.random.fold_in(_rk, 511), 0.3 * jnp.ones((16,), jnp.float32), (32, 64))
        _ctx_4096t = jnp.einsum('bsk,bkd->bsd', _ctx_4096c, _ctx_4096P)
        _ctx_4096t = _ctx_4096t * jax.lax.rsqrt(jnp.mean(jnp.square(_ctx_4096t)) + 1e-12) * 0.953939
        ctx_4096 = -2.8382e-05 + 0.999851 * (_ctx_4096t + 0.3 * jax.random.normal(jax.random.fold_in(_rk, 611), (32, 64, 512), jnp.float32))
        _validS = jnp.arange(64)[None, :] < _lenS[:, None]
        _validS2 = jnp.arange(64)[None, :] < _lenS2[:, None]
        _causal = jnp.tril(jnp.ones((64, 64), dtype=bool))
        mask_1x1xSxS2_ff0 = jnp.where(jnp.ones((1, 1, 64, 64), dtype=bool), 0.0, -1000000000.0).astype(jnp.float32)
        return (x, ctx_4096, mask_1x1xSxS2_ff0)
    x, ctx_4096, mask_1x1xSxS2_ff0 = _rec_inputs()

    def _L0_attn_setup():
        import jax, jax.numpy as jnp
        import numpy as np
        B, S, D = (2, 256, 512)
        NH, NKV = (32, 8)
        HD = D // NH
        NREP = NH // NKV
        SCALE = HD ** (-0.5)
        key = jax.random.key(seed)
        kx, kq, kk, kv, ko = jax.random.split(key, 5)
        s = 0.02
        return {'x': jax.random.normal(kx, (B, S, D), dtype=jnp.float32), 'wq': jax.random.normal(kq, (D, NH * HD), dtype=jnp.float32) * s, 'wk': jax.random.normal(kk, (D, NKV * HD), dtype=jnp.float32) * s, 'wv': jax.random.normal(kv, (D, NKV * HD), dtype=jnp.float32) * s, 'wo': jax.random.normal(ko, (NH * HD, D), dtype=jnp.float32) * s}
    _L0_attn_all = _L0_attn_setup()
    _L0_attn_in = {k: v for k, v in _L0_attn_all.items() if k in ('wq', 'wk', 'wv', 'wo')}
    del _L0_attn_all

    def _L0_xattn_setup():
        import jax, jax.numpy as jnp
        import numpy as np
        B, Q, K, D = (1, 128, 6404, 512)
        H, KVH, HD = (32, 8, 128)
        GROUPS = H // KVH
        EPS = 1e-05

        def _rmsnorm(x, w):
            xf = x.astype(jnp.float32)
            var = jnp.mean(xf * xf, axis=-1, keepdims=True)
            return (xf * jax.lax.rsqrt(var + EPS)).astype(x.dtype) * w
        key = jax.random.key(seed)
        ks = jax.random.split(key, 8)
        s = 0.02
        return {'hidden_states': jax.random.normal(ks[0], (B, Q, D), jnp.float32), 'cross_attention_states': jax.random.normal(ks[1], (B, K, D), jnp.float32), 'attention_mask': jnp.zeros((B, 1, Q, K), jnp.float32), 'Wq': jax.random.normal(ks[2], (H * HD, D), jnp.float32) * s, 'Wk': jax.random.normal(ks[3], (KVH * HD, D), jnp.float32) * s, 'Wv': jax.random.normal(ks[4], (KVH * HD, D), jnp.float32) * s, 'Wo': jax.random.normal(ks[5], (D, H * HD), jnp.float32) * s, 'q_norm_w': jnp.ones((HD,), jnp.float32), 'k_norm_w': jnp.ones((HD,), jnp.float32)}
    _L0_xattn_all = _L0_xattn_setup()
    _L0_xattn_in = {k: v for k, v in _L0_xattn_all.items() if k in ('Wq', 'Wk', 'Wv', 'Wo', 'q_norm_w', 'k_norm_w')}
    del _L0_xattn_all

    def _L0_ffn_setup():
        import jax, jax.numpy as jnp
        import numpy as np
        HID, INT, LAT, NE, K = (512, 1024, 256, 8, 2)
        LN_EPS = 1e-05

        def _layernorm(x, gamma, beta):
            mu = jnp.mean(x, axis=-1, keepdims=True)
            var = jnp.var(x, axis=-1, keepdims=True)
            return (x - mu) * jax.lax.rsqrt(var + LN_EPS) * gamma + beta
        key = jax.random.key(seed)
        ks = jax.random.split(key, 8)
        s = lambda d: 1.0 / np.sqrt(d)
        return {'hidden_states': jax.random.normal(ks[0], (4, 256, HID), jnp.float32), 'gate_w': jax.random.normal(ks[1], (HID, NE), jnp.float32) * s(HID), 'up_w': jax.random.normal(ks[2], (HID, INT), jnp.float32) * s(HID), 'down_w': jax.random.normal(ks[3], (INT, HID), jnp.float32) * s(INT), 'fc1_w': jax.random.normal(ks[4], (HID, LAT), jnp.float32) * s(HID), 'fc2_w': jax.random.normal(ks[5], (LAT, HID), jnp.float32) * s(LAT), 'expert_w': jax.random.normal(ks[6], (LAT, LAT), jnp.float32), 'ln_gamma': jnp.ones((HID,), jnp.float32), 'ln_beta': jnp.zeros((HID,), jnp.float32)}
    _L0_ffn_all = _L0_ffn_setup()
    _L0_ffn_in = {k: v for k, v in _L0_ffn_all.items() if k in ('gate_w', 'up_w', 'down_w', 'fc1_w', 'fc2_w', 'expert_w', 'ln_gamma', 'ln_beta')}
    del _L0_ffn_all
    return {'x': x, 'ctx_4096': ctx_4096, 'mask_1x1xSxS2_ff0': mask_1x1xSxS2_ff0, 'L0_attn_wq': _L0_attn_in['wq'], 'L0_attn_wk': _L0_attn_in['wk'], 'L0_attn_wv': _L0_attn_in['wv'], 'L0_attn_wo': _L0_attn_in['wo'], 'L0_xattn_Wq': _L0_xattn_in['Wq'], 'L0_xattn_Wk': _L0_xattn_in['Wk'], 'L0_xattn_Wv': _L0_xattn_in['Wv'], 'L0_xattn_Wo': _L0_xattn_in['Wo'], 'L0_xattn_q_norm_w': _L0_xattn_in['q_norm_w'], 'L0_xattn_k_norm_w': _L0_xattn_in['k_norm_w'], 'L0_ffn_gate_w': _L0_ffn_in['gate_w'], 'L0_ffn_up_w': _L0_ffn_in['up_w'], 'L0_ffn_down_w': _L0_ffn_in['down_w'], 'L0_ffn_fc1_w': _L0_ffn_in['fc1_w'], 'L0_ffn_fc2_w': _L0_ffn_in['fc2_w'], 'L0_ffn_expert_w': _L0_ffn_in['expert_w'], 'L0_ffn_ln_gamma': _L0_ffn_in['ln_gamma'], 'L0_ffn_ln_beta': _L0_ffn_in['ln_beta']}

def reference(x, ctx_4096, mask_1x1xSxS2_ff0, L0_attn_wq, L0_attn_wk, L0_attn_wv, L0_attn_wo, L0_xattn_Wq, L0_xattn_Wk, L0_xattn_Wv, L0_xattn_Wo, L0_xattn_q_norm_w, L0_xattn_k_norm_w, L0_ffn_gate_w, L0_ffn_up_w, L0_ffn_down_w, L0_ffn_fc1_w, L0_ffn_fc2_w, L0_ffn_expert_w, L0_ffn_ln_gamma, L0_ffn_ln_beta):
    import jax
    import jax.numpy as jnp

    def _L0_attn_ref(x, wq, wk, wv, wo):
        import jax, jax.numpy as jnp
        import numpy as np
        B, S, D = (2, 256, 512)
        NH, NKV = (32, 8)
        HD = D // NH
        NREP = NH // NKV
        SCALE = HD ** (-0.5)
        b, s, _ = x.shape
        q = (x @ wq).reshape(b, s, NH, HD)
        k = (x @ wk).reshape(b, s, NKV, HD)
        v = (x @ wv).reshape(b, s, NKV, HD)
        k = jnp.repeat(k, NREP, axis=2)
        v = jnp.repeat(v, NREP, axis=2)
        scores = jnp.einsum('bihd,bjhd->bhij', q, k) * SCALE
        causal = jnp.tril(jnp.ones((s, s), dtype=bool))
        scores = jnp.where(causal, scores, jnp.finfo(scores.dtype).min)
        attn = jax.nn.softmax(scores, axis=-1)
        out = jnp.einsum('bhij,bjhd->bihd', attn, v)
        out = out.reshape(b, s, NH * HD)
        return out @ wo

    def _L0_xattn_ref(hidden_states, cross_attention_states, attention_mask, Wq, Wk, Wv, Wo, q_norm_w, k_norm_w):
        import jax, jax.numpy as jnp
        import numpy as np
        B, Q, K, D = (1, 128, 6404, 512)
        H, KVH, HD = (32, 8, 128)
        GROUPS = H // KVH
        EPS = 1e-05

        def _rmsnorm(x, w):
            xf = x.astype(jnp.float32)
            var = jnp.mean(xf * xf, axis=-1, keepdims=True)
            return (xf * jax.lax.rsqrt(var + EPS)).astype(x.dtype) * w
        bsz, q_len, _ = hidden_states.shape
        kv_len = cross_attention_states.shape[1]
        q = (hidden_states @ Wq.T).reshape(bsz, q_len, H, HD).transpose(0, 2, 1, 3)
        k = (cross_attention_states @ Wk.T).reshape(bsz, kv_len, KVH, HD).transpose(0, 2, 1, 3)
        v = (cross_attention_states @ Wv.T).reshape(bsz, kv_len, KVH, HD).transpose(0, 2, 1, 3)
        q = _rmsnorm(q, q_norm_w)
        k = jnp.repeat(k, GROUPS, axis=1)
        v = jnp.repeat(v, GROUPS, axis=1)
        k = _rmsnorm(k, k_norm_w)
        scale = 1.0 / np.sqrt(HD)
        scores = jnp.einsum('bhqd,bhkd->bhqk', q, k) * scale
        scores = scores + attention_mask[:, :, :, :kv_len]
        probs = jax.nn.softmax(scores.astype(jnp.float32), axis=-1).astype(q.dtype)
        out = jnp.einsum('bhqk,bhkd->bhqd', probs, v)
        out = out.transpose(0, 2, 1, 3).reshape(bsz, q_len, H * HD)
        return out @ Wo.T

    def _L0_ffn_ref(hidden_states, gate_w, up_w, down_w, fc1_w, fc2_w, expert_w, ln_gamma, ln_beta):
        import jax, jax.numpy as jnp
        import numpy as np
        HID, INT, LAT, NE, K = (512, 1024, 256, 8, 2)
        LN_EPS = 1e-05

        def _layernorm(x, gamma, beta):
            mu = jnp.mean(x, axis=-1, keepdims=True)
            var = jnp.var(x, axis=-1, keepdims=True)
            return (x - mu) * jax.lax.rsqrt(var + LN_EPS) * gamma + beta
        logits = jnp.einsum('bsh,he->bse', hidden_states, gate_w)
        routing_weights, selected_experts = jax.lax.top_k(logits, K)
        h = jax.nn.relu(jnp.einsum('bsh,hi->bsi', hidden_states, up_w)) ** 2
        shared_out = jnp.einsum('bsi,ih->bsh', h, down_w)
        x_latent = jnp.einsum('bsh,hl->bsl', hidden_states, fc1_w)
        expert_out = jnp.einsum('bsl,lm->bsm', x_latent, expert_w)
        moe_out = expert_out * jnp.sum(routing_weights, axis=-1, keepdims=True)
        routed_out = jnp.einsum('bsl,lh->bsh', moe_out, fc2_w)
        return _layernorm(shared_out + routed_out, ln_gamma, ln_beta)
    x = x + _L0_attn_ref(_layernorm(x, axis=-1), L0_attn_wq, L0_attn_wk, L0_attn_wv, L0_attn_wo)
    x = x + _L0_xattn_ref(_layernorm(x, axis=-1), ctx_4096, mask_1x1xSxS2_ff0, L0_xattn_Wq, L0_xattn_Wk, L0_xattn_Wv, L0_xattn_Wo, L0_xattn_q_norm_w, L0_xattn_k_norm_w)
    x = x + _L0_ffn_ref(_layernorm(x, axis=-1), L0_ffn_gate_w, L0_ffn_up_w, L0_ffn_down_w, L0_ffn_fc1_w, L0_ffn_fc2_w, L0_ffn_expert_w, L0_ffn_ln_gamma, L0_ffn_ln_beta)
    return x

_drawn_inputs = setup_inputs


def setup_inputs(seed=0):
    import zlib

    import numpy as np

    out = dict(_drawn_inputs(seed))
    spreads = {'L0_xattn_q_norm_w': (1.0, 0.593),
     'L0_xattn_k_norm_w': (1.0, 0.588),
     'L0_ffn_ln_gamma': (1.0, 0.2),
     'L0_ffn_ln_beta': (0.0, 0.1)}
    factors = {'L0_attn_wq': 5.67, 'L0_attn_wk': 4.879}
    for name, (base, spread) in spreads.items():
        noise = np.random.default_rng([zlib.crc32(name.encode()), seed]).standard_normal(out[name].shape)
        drawn = base * np.exp(spread * noise) if base else spread * noise
        out[name] = jnp.asarray(drawn.astype(out[name].dtype))
    for name, factor in factors.items():
        out[name] = (out[name] * factor).astype(out[name].dtype)
    return out
```

```python
from contextlib import ExitStack

import numpy as np

import concourse.bass as bass
from concourse import mybir

F32 = mybir.dt.float32
FR = mybir.dt.float32r
ALU = mybir.AluOpType
ACT = mybir.ActivationFunctionType
AX_X = mybir.AxisListType.X

P = 128
D = 512
KC = D // P
SEQ = 64
BATCH = 32
HALVES = 2
HALF = BATCH * SEQ // HALVES
NT = HALF // P
NSEQ = HALF // SEQ
NG = 8
REP = 4
HD1 = 16
HD2 = 128
INNER = 1024
LAT = 256
NE = 8
EPS = 1e-5
COLS = 512

UNITS1 = NSEQ * 2
CHUNKS = NT // 2
ACC1 = 4 * NT + 6
ACC2 = 22
ACC3 = NT + 7 * CHUNKS
LEAD = 2
PRING = 4
W_KV, W_Q, W_O, W_OT = 0, 1024, 3072, 5120
W_H = 4096


class Count:

    def __init__(self, sem, n0, n1, n2, n3, by=1):
        self.sem, self.n0, self.n1, self.n2, self.n3, self.by = sem, n0, n1, n2, n3, by


class Place:

    def __init__(self, stage, half, turn=None):
        self.stage, self.half, self.turn = stage, half, turn

    def at(self, c, k):
        value = c.n0 + k
        if self.stage > 1:
            value += c.n1
        if self.stage > 2:
            value += NG * c.n2
        value = self.half * (c.by * (c.n1 + NG * c.n2 + c.n3)) + c.by * value
        if self.stage == 2 and c.n2:
            value = value + self.turn * (c.by * c.n2)
        return value


def decoder_block(nc, x_in, ctx_in, mask_in, w_self, w_cross, qn_in, kn_in, w_ffn,
                  f1g_in, expt_in, fc2_in, gamma_in, beta_in, out):
    with ExitStack() as stack:
        def sb(name, shape, dt=F32):
            return stack.enter_context(nc.sbuf_tensor(name, shape, dt))

        def bank(name):
            return stack.enter_context(nc.psum_tensor(name, [P, COLS], F32))

        credited = []

        def count(name, n0, n1, n2, n3, by=1):
            c = Count(stack.enter_context(nc.semaphore(name)), n0, n1, n2, n3, by)
            if n0:
                credited.append(c)
            return c

        x = sb("x", [P, NT, D])
        xn_hi, xn_lo = sb("xn_hi", [P, KC, HALF], FR), sb("xn_lo", [P, KC, HALF], FR)
        cx_hi, cx_lo = sb("cx_hi", [P, KC, HALF], FR), sb("cx_lo", [P, KC, HALF], FR)
        dn_hi = cx_hi[:].rearrange("p k t -> p (k t)")
        dn_lo = cx_lo[:].rearrange("p k t -> p (k t)")
        w_hi, w_lo = sb("w_hi", [P, 6144], FR), sb("w_lo", [P, 6144], FR)
        stage = sb("stage", [P, 2, 1024])
        qb = sb("qb", [P, 4096])
        kraw = sb("kraw", [P, NT, P])
        ctile = kraw[:].rearrange("p t d -> p (t d)").rearrange("p (r d) -> p r d", r=2)
        kt = sb("kt", [P, HALF])
        vraw = sb("vraw", [P, NT, P])
        zone = sb("zone", [P, 2048])
        vbd = zone[:, 0:1024].rearrange("p (r i c) -> p r i c", r=2, i=4)
        kbd = zone[:, 1024:2048].rearrange("p (r g k) -> p r g k", r=2, g=NG)
        vpad = zone[:].rearrange("p (t b d) -> p t b d", t=NT, b=2)
        prob = sb("prob", [P, PRING, COLS])
        probt = sb("probt", [P, 2, COLS])
        xn = sb("xn", [P, 2, D])
        w23_hi, w23_lo = sb("w23_hi", [P, 2, D], FR), sb("w23_lo", [P, 2, D], FR)
        f1g_hi, f1g_lo = sb("f1g_hi", [P, KC, LAT + NE], FR), sb("f1g_lo", [P, KC, LAT + NE], FR)
        gamma, beta = sb("gamma", [P, D]), sb("beta", [P, D])
        latt_hi, latt_lo = sb("latt_hi", [P, 2, 2 * P], FR), sb("latt_lo", [P, 2, 2 * P], FR)
        scrap = sb("scrap", [P, 2])
        squares = sb("squares", [P, 2, REP, P], mybir.dt.bfloat16)
        ident = sb("ident", [P, P])
        causal, mask = sb("causal", [P, SEQ]), sb("mask", [P, SEQ])
        gsel = sb("gsel", [P, NG])
        qkn = sb("qkn", [P, 4])
        mhalf = sb("mhalf", [P, 16])
        bn = sb("bn", [P, NT, 6])
        mv = sb("mv", [P, NT, 2])
        veps, rstd = sb("veps", [P, NT]), sb("rstd", [P, NT])
        kss, kve, krs = sb("kss", [P, NT]), sb("kve", [P, NT]), sb("krs", [P, NT])
        qss, qve, qrs = sb("qss", [P, 2, 2, REP]), sb("qve", [P, 2, 2 * REP]), sb("qrs", [P, 2, 2 * REP])
        pmax, psum_, prec = (sb(n, [P, PRING, 8]) for n in ("pmax", "psum_", "prec"))
        top8, route = sb("top8", [P, 2, 8]), sb("route", [P, 2])
        ybn, ymv, yve, yrs = sb("ybn", [P, 2, 6]), sb("ymv", [P, 2, 2]), sb("yve", [P, 2]), sb("yrs", [P, 2])

        q1t = qb[:].rearrange("p (b r q) -> p b r q", r=REP, q=SEQ)
        q2t = qb[:, 0:2048].rearrange("p (c t b h q) -> p c t b h q", c=2, t=2, b=2, h=REP)
        qraw = qb[:, 2048:4096].rearrange("p (t h d) -> p t h d", t=4, h=REP)
        relu = qb[:, 0:1024].rearrange("p (r n) -> p r n", r=2)
        hsq = qb[:, 1024:2048].rearrange("p (r n) -> p r n", r=2)
        latn = qb[:, 2048:2560].rearrange("p (t l) -> p t l", t=2)
        znorm = qb[:, 2560:3584].rearrange("p (r n) -> p r n", r=2)
        f1g_raw = qb[:, 0:KC * (LAT + NE)].rearrange("p (k n) -> p k n", k=KC)
        expt_raw = qb[:, 1056:1568].rearrange("p (m l) -> p m l", m=2)
        fc2_raw = qb[:, 1568:2592].rearrange("p (m n) -> p m n", m=2)
        ot_hi = w_hi[:, W_OT:W_OT + 1024].rearrange("p (r n) -> p r n", r=2)
        ot_lo = w_lo[:, W_OT:W_OT + 1024].rearrange("p (r n) -> p r n", r=2)
        ht_hi = w_hi[:, W_H:W_H + 2048].rearrange("p (f t) -> p f t", f=INNER // P)
        ht_lo = w_lo[:, W_H:W_H + 2048].rearrange("p (f t) -> p f t", f=INNER // P)

        acc = [bank("acc0"), bank("acc1")]
        sc = bank("sc")
        pt = bank("pt")
        ot = [bank("ot0"), bank("ot1")]
        y = [bank("y0"), bank("y1")]

        const_step = count("const_step", 0, 0, 0, 0)
        const_ld, const_made, wqk_made, w23_rdy, w23_hi_done, w23_lo_done, f1g_hi_done, f1g_lo_done = (
            count(n, 0, 0, 0, 0) for n in ("const_ld", "const_made", "wqk_made", "w23_rdy", "w23_hi_done",
                                           "w23_lo_done", "f1g_hi_done", "f1g_lo_done"))
        x_ld = [count(f"x_ld{i}", 0, 1, 0, 0, by=16) for i in range(4)]
        x_st = [count(f"x_st{i}", 1, 0, 0, 1, by=16) for i in range(NT)]
        ctx_ld = [count(f"ctx_ld{i}", 0, NT // 2, 0, 0, by=16) for i in range(2)]
        w_ld = [count(f"w_ld{i}", 0, 3, 3, 4, by=16) for i in range(2)]
        w_hi_done = count("w_hi_done", 0, 6, 6, 8)
        w_lo_done = count("w_lo_done", 2, 6, 6, 8)
        zone_clear = count("zone_clear", 0, 2, 0, 0)
        acc_rdy = count("acc_rdy", 1, ACC1, ACC2, ACC3)
        acc_free = [count(f"acc_free{i}", 1, ACC1 // 2, ACC2 // 2, ACC3 // 2) for i in range(2)]
        ctx_hi_done = count("ctx_hi_done", 0, NT, 0, 0)
        ln_bn, ln_aggr, ln_veps, ln_rstd, ln_xn, ln_hi_done = (
            count(n, 0, 2 * NT, 0, NT) for n in ("ln_bn", "ln_aggr", "ln_veps", "ln_rstd", "ln_xn", "ln_hi_done"))
        kv_act = count("kv_act", 0, 0, 4, 0)
        k_ve, k_rs, k_nrm = (count(n, 0, 0, 1, 0) for n in ("k_ve", "k_rs", "k_nrm"))
        q_ve, q_rs, q_nrm = (count(n, 0, 0, CHUNKS, 0) for n in ("q_ve", "q_rs", "q_nrm"))
        kbd_done = count("kbd_done", 0, NSEQ, 0, 0)
        vbd_done = count("vbd_done", 0, NSEQ, 0, 0)
        pv_done = count("pv_done", 0, UNITS1, 0, 0)
        ot_rdy = count("ot_rdy", 0, 0, NT, 0)
        sc_rdy, s_add, s_max, s_sub, s_exp, s_sum, s_rec, s_nrm, pt_rdy, pt_done = (
            count(n, 1, UNITS1, CHUNKS, 0) for n in ("sc_rdy", "s_add", "s_max", "s_sub", "s_exp", "s_sum",
                                                     "s_rec", "s_nrm", "pt_rdy", "pt_done"))
        ot_hi_done = count("ot_hi_done", 0, NT, NT, 0)
        ot_lo_done = count("ot_lo_done", 2, NT, NT, 0)
        y_rdy = count("y_rdy", 1, NT, NT, NT)
        y_free = count("y_free", 2, NT, NT, NT)
        hsq_done, ht_hi_done, ht_lo_done = (
            count(n, 0, 0, 0, 4 * CHUNKS) for n in ("hsq_done", "ht_hi_done", "ht_lo_done"))
        latt_hi_done = count("latt_hi_done", 0, 0, 0, CHUNKS)
        top_done, route_done, y_bn, y_aggr, y_ve, y_rs, xb_done, x_out = (
            count(n, 0, 0, 0, NT) for n in ("top_done", "route_done", "y_bn", "y_aggr", "y_ve", "y_rs",
                                            "xb_done", "x_out"))

        block = stack.enter_context(nc.Block())

        A1_CTX, A1_LN1, A1_KV, A1_Q, A1_KT, A1_LN2 = 0, NT, 2 * NT, 2 * NT + 4, 3 * NT + 4, 3 * NT + 6
        A2_KV, A2_KT = 0, 8
        A2_QP = [4, 5, 6, 7, 12, 13, 16, 17]
        A2_QT = [10, 11, 14, 15, 18, 19, 20, 21]
        A3_LN, A3_UP, A3_LAT, A3_LATT = 0, NT, NT + 4, NT + 6

        PIECES = [(W_KV, 512), (W_KV + 512, 512), (W_Q, 1024), (W_Q + 1024, 1024), (W_O, 1024), (W_O + 1024, 1024)]

        def piece_target(stage_no, n, part):
            if stage_no < 3:
                at, width = PIECES[n]
                return (w_hi, w_lo)[part][:, at:at + width], width
            if n < 4:
                return (dn_hi, dn_lo)[part][:, n * 1024:(n + 1) * 1024], 1024
            return (w_hi, w_lo)[part][:, (n - 4) * 1024:(n - 3) * 1024], 1024

        def evacuated(eng, at, n):
            eng.wait_ge(acc_free[n % 2].sem, at(acc_free[n % 2], n // 2 + 1))

        def tile_of(a, i):
            return a[:, :, i * P:(i + 1) * P]

        def carry_wait_dve():
            nc.vector.memset(scrap[:, 0:1], 0.0)

        def carry_wait_pool():
            nc.gpsimd.tensor_tensor(scrap[:, 1:2], mhalf[:, 0:1], mhalf[:, 0:1], ALU.mult)

        def blocks(columns):
            return columns[:].rearrange("p (k t) -> p k t", k=4)

        def by_sequence(columns):
            return columns.rearrange("p (b h q) -> p b h q", b=2, h=REP)

        def by_head(columns):
            return columns.rearrange("p (h b q) -> p b h q", b=2, h=REP)

        def spread(small, count_, width):
            return small.unsqueeze(2).to_broadcast([P, count_, width])

        def own_block(r, g2):
            base = vbd[g2 * SEQ:(g2 + 1) * SEQ, r, 0, g2 * HD1:(g2 + 1) * HD1]
            return bass.AP(tensor=base.tensor, offset=base.offset, ap=[base.ap[0], [P + 2 * HD1, 4], [1, HD1]])

        @block.sync
        def _(sp):
            for c in credited:
                sp.sem_inc(c.sem, c.n0 * c.by)
            sp.dma_start(qkn[:, 0:1], qn_in).then_inc(const_ld.sem, 16)
            sp.dma_start(qkn[:, 1:2], kn_in).then_inc(const_ld.sem, 16)
            sp.dma_start(mask[0:SEQ, :], mask_in).then_inc(const_ld.sem, 16)
            sp.dma_start(mask[SEQ:P, :], mask_in).then_inc(const_ld.sem, 16)
            sp.dma_start(f1g_raw, f1g_in).then_inc(const_ld.sem, 16)
            sp.dma_start(expt_raw, expt_in).then_inc(const_ld.sem, 16)
            sp.dma_start(fc2_raw, fc2_in).then_inc(const_ld.sem, 16)
            sp.dma_start(gamma[:], gamma_in.to_broadcast([P, D])).then_inc(const_ld.sem, 16)
            sp.dma_start(beta[:], beta_in.to_broadcast([P, D])).then_inc(const_ld.sem, 16)

            def load_piece(at, source, n):
                sp.wait_ge(w_lo_done.sem, at(w_lo_done, n - 1))
                width = source.shape[-1]
                sp.dma_start(stage[:, n % 2, 0:width], source).then_inc(w_ld[n % 2].sem, 16)

            def load_attention_pieces(at, source, which):
                for n in which:
                    column, width = PIECES[n]
                    load_piece(at, source[:, column:column + width], n)

            with sp.Fori(0, HALVES) as half:
                at = Place(1, half).at
                x_half = x_in[bass.ds(half, 1)].rearrange("o t p d -> (o p) t d")
                c_half = ctx_in[bass.ds(half, 1)].rearrange("o t p d -> (o p) t d")

                def load_ctx(i):
                    if i < 2:
                        sp.wait_ge(acc_rdy.sem, at(acc_rdy, 0))
                    else:
                        sp.wait_ge(acc_rdy.sem, at(acc_rdy, A1_CTX + i - 1))
                    sp.dma_start(ctile[:, i % 2, :], c_half[:, i, :]).then_inc(ctx_ld[i % 2].sem, 16)

                def load_x(i):
                    for t in (2 * i, 2 * i + 1):
                        sp.wait_ge(x_st[t].sem, at(x_st[t], 0))
                    sp.dma_start(x[:, 2 * i:2 * i + 2, :], x_half[:, 2 * i:2 * i + 2, :]).then_inc(x_ld[i].sem, 16)

                load_ctx(0)
                load_ctx(1)
                load_x(0)
                load_x(1)
                load_ctx(2)
                load_ctx(3)
                load_x(2)
                load_x(3)
                load_attention_pieces(at, w_self, range(2))
                for i in range(4, NT):
                    load_ctx(i)
                load_attention_pieces(at, w_self, range(2, 6))
                with sp.Fori(0, NG) as turn:
                    load_attention_pieces(Place(2, half, turn).at,
                                          w_cross[bass.ds(turn, 1)].rearrange("o p n -> (o p) n"), range(6))
                at = Place(3, half).at
                for n in range(8):
                    load_piece(at, w_ffn[n], n)
                out_half = out[bass.ds(half, 1)].rearrange("o t p d -> (o p) t d")
                for t in range(NT):
                    sp.wait_ge(x_out.sem, at(x_out, t + 1))
                    sp.dma_start(out_half[:, t, :], x[:, t, :]).then_inc(x_st[t].sem, 16)
            for t in range(NT):
                sp.wait_ge(x_st[t].sem, 16 * (HALVES + 1))

        @block.tensor
        def _(pe):
            def split_mm(target, l_hi, l_lo, r_hi, r_lo, first, last):
                nc.tensor.matmul(target, l_hi, r_hi, start=first, stop=False)
                nc.tensor.matmul(target, l_hi, r_lo, start=False, stop=False)
                return nc.tensor.matmul(target, l_lo, r_hi, start=False, stop=last)

            def acc_bank(at, n):
                pe.wait_ge(acc_free[n % 2].sem, at(acc_free[n % 2], n // 2))
                return acc[n % 2]

            def pieces_split(at, n):
                pe.wait_ge(w_hi_done.sem, at(w_hi_done, n))
                pe.wait_ge(w_lo_done.sem, at(w_lo_done, n))

            def transpose_tile(at, n, source):
                to = acc_bank(at, n)
                for k in range(4):
                    ins = nc.tensor.transpose(to[:, k * P:(k + 1) * P], source[:, k * P:(k + 1) * P], ident[:])
                ins.then_inc(acc_rdy.sem, 1)

            def layernorm_tiles(at, base, first):
                for i in range(NT):
                    pe.wait_ge(ln_xn.sem, at(ln_xn, first + i + 1))
                    transpose_tile(at, base + i, xn[:, i % 2, :])

            def project_kv(at, base, a_hi, a_lo):
                pieces_split(at, 2)
                for m in range(NT // 2):
                    to = acc_bank(at, base + m)
                    for t in range(2):
                        i = 2 * m + t
                        for k in range(KC):
                            w = slice(W_KV + k * 256, W_KV + (k + 1) * 256)
                            ins = split_mm(to[:, t * 256:(t + 1) * 256],
                                           a_hi[:, k, i * P:(i + 1) * P], a_lo[:, k, i * P:(i + 1) * P],
                                           w_hi[:, w], w_lo[:, w], k == 0, k == KC - 1)
                    ins.then_inc(acc_rdy.sem, 1)

            def transpose_keys(at, base):
                keys = kraw[:].rearrange("p t d -> p (t d)")
                for m in range(2):
                    transpose_tile(at, base + m, keys[:, m * COLS:(m + 1) * COLS])

            def transpose_probs(at, u):
                pe.wait_ge(s_nrm.sem, at(s_nrm, u + 1))
                pe.wait_ge(pt_done.sem, at(pt_done, u))
                for k in range(4):
                    ins = nc.tensor.transpose(pt[:, k * P:(k + 1) * P], prob[:, u % PRING, k * P:(k + 1) * P], ident[:])
                ins.then_inc(pt_rdy.sem, 1)

            def project_out(at, i):
                pe.wait_ge(ot_hi_done.sem, at(ot_hi_done, i + 1))
                pe.wait_ge(ot_lo_done.sem, at(ot_lo_done, i + 1))
                pe.wait_ge(y_free.sem, at(y_free, i - 1))
                if i == 0:
                    pieces_split(at, 6)
                hi, lo = (blocks(o[:, i % 2, :]) for o in (ot_hi, ot_lo))
                for h in range(REP):
                    w = slice(W_O + h * D, W_O + (h + 1) * D)
                    ins = split_mm(y[i % 2][:], hi[:, h], lo[:, h], w_hi[:, w], w_lo[:, w], h == 0, h == REP - 1)
                ins.then_inc(y_rdy.sem, 1)

            pe.wait_ge(const_ld.sem, 16 * 9)
            pe.wait_ge(const_made.sem, 1)
            pe.wait_ge(f1g_lo_done.sem, 1)
            for l in range(2):
                for m in range(2):
                    ins = nc.tensor.matmul(y[l][:], expt_raw[:, m, l * P:(l + 1) * P], fc2_raw[:, m, :],
                                           start=m == 0, stop=m == 1)
                ins.then_inc(w23_rdy.sem, 1)
            pe.wait_ge(w23_lo_done.sem, 2)

            with pe.Fori(0, HALVES) as half:
                at = Place(1, half).at
                for i in range(NT):
                    pe.wait_ge(ctx_ld[i % 2].sem, at(ctx_ld[i % 2], i // 2 + 1))
                    transpose_tile(at, A1_CTX + i, ctile[:, i % 2, :])
                layernorm_tiles(at, A1_LN1, 0)
                evacuated(pe, at, A1_LN1 + NT - 2)
                evacuated(pe, at, A1_LN1 + NT - 1)
                project_kv(at, A1_KV, xn_hi, xn_lo)
                pieces_split(at, 4)
                for s in range(2):
                    for r in range(REP):
                        n = s * REP + r
                        to = acc_bank(at, A1_Q + n)
                        for k in range(KC):
                            w = slice(W_Q + k * D + r * P, W_Q + k * D + (r + 1) * P)
                            ins = split_mm(to[:], w_hi[:, w], w_lo[:, w],
                                           xn_hi[:, k, s * COLS:(s + 1) * COLS], xn_lo[:, k, s * COLS:(s + 1) * COLS],
                                           k == 0, k == KC - 1)
                        ins.then_inc(acc_rdy.sem, 1)
                transpose_keys(at, A1_KT)

                def scores1(u):
                    b, rp = u // 2, u % 2
                    if u == 0:
                        evacuated(pe, at, A1_Q + 6)
                        evacuated(pe, at, A1_Q + 7)
                    pe.wait_ge(kbd_done.sem, at(kbd_done, b + 1))
                    pe.wait_ge(s_add.sem, at(s_add, u))
                    nc.tensor.matmul(sc[:], q1t[:, b, 2 * rp:2 * rp + 2, :].rearrange("p r q -> p (r q)"),
                                     kbd[:, b % 2].rearrange("p g k -> p (g k)"), start=True, stop=True
                                     ).then_inc(sc_rdy.sem, 1)

                def values1(u):
                    b, rp = u // 2, u % 2
                    i = b // 2
                    pe.wait_ge(pt_done.sem, at(pt_done, u + 1))
                    pe.wait_ge(vbd_done.sem, at(vbd_done, b + 1))
                    if u % 4 == 0:
                        pe.wait_ge(ot_lo_done.sem, at(ot_lo_done, i - 1))
                    column = (b % 2) * 256 + rp * P
                    for k in range(4):
                        ins = nc.tensor.matmul(ot[i % 2][:, column:column + P], vbd[:, b % 2, k, :],
                                               probt[:, u % 2, k * P:(k + 1) * P], start=k == 0, stop=k == 3)
                    ins.then_inc(pv_done.sem, 1)

                for u in range(LEAD):
                    scores1(u)
                for u in range(UNITS1 + 3):
                    if u + LEAD < UNITS1:
                        scores1(u + LEAD)
                    if u < UNITS1:
                        transpose_probs(at, u)
                    if 1 <= u <= UNITS1:
                        values1(u - 1)
                    if u >= 6 and u % 4 == 2:
                        project_out(at, (u - 6) // 4)
                layernorm_tiles(at, A1_LN2, NT)

                with pe.Fori(0, NG) as turn:
                    at = Place(2, half, turn).at

                    def queries(i):
                        to = acc_bank(at, A2_QP[i])
                        for k in range(KC):
                            w = slice(W_Q + k * D, W_Q + (k + 1) * D)
                            ins = split_mm(to[:], xn_hi[:, k, i * P:(i + 1) * P], xn_lo[:, k, i * P:(i + 1) * P],
                                           w_hi[:, w], w_lo[:, w], k == 0, k == KC - 1)
                        ins.then_inc(acc_rdy.sem, 1)

                    def transpose_queries(c):
                        pe.wait_ge(q_nrm.sem, at(q_nrm, c + 1))
                        for i in (2 * c, 2 * c + 1):
                            transpose_tile(at, A2_QT[i], qraw[:, i % 4].rearrange("p h d -> p (h d)"))

                    def scores2(c):
                        evacuated(pe, at, A2_QT[2 * c])
                        evacuated(pe, at, A2_QT[2 * c + 1])
                        pe.wait_ge(s_add.sem, at(s_add, c))
                        for t in range(2):
                            for j in range(2):
                                for b in range(2):
                                    column = ((t * 2 + j) * 2 + b) * SEQ
                                    token = t * P + b * SEQ
                                    ins = nc.tensor.matmul(
                                        sc[:, column:column + SEQ],
                                        q2t[:, c % 2, t, b, 2 * j:2 * j + 2, :].rearrange("p h q -> p (h q)"),
                                        kt[:, 2 * c * P + token:2 * c * P + token + SEQ], start=True, stop=True)
                        ins.then_inc(sc_rdy.sem, 1)

                    def values2(c):
                        pe.wait_ge(pt_done.sem, at(pt_done, c + 1))
                        for t in range(2):
                            i = 2 * c + t
                            pe.wait_ge(ot_lo_done.sem, at(ot_lo_done, i - 1))
                            for b in range(2):
                                ins = nc.tensor.matmul(ot[t][:, b * 256:(b + 1) * 256], vpad[:, i, b, :],
                                                       probt[:, c % 2, t * 256:(t + 1) * 256], start=True, stop=True)
                            ins.then_inc(ot_rdy.sem, 1)

                    for b in range(2):
                        pe.wait_ge(acc_free[b].sem, at(acc_free[b], 0))
                    project_kv(at, A2_KV, cx_hi, cx_lo)
                    pieces_split(at, 4)
                    for i in range(4):
                        queries(i)
                    pe.wait_ge(k_nrm.sem, at(k_nrm, 1))
                    transpose_keys(at, A2_KT)
                    transpose_queries(0)
                    queries(4)
                    scores2(0)
                    queries(5)
                    transpose_queries(1)
                    queries(6)
                    scores2(1)
                    transpose_probs(at, 0)
                    queries(7)
                    values2(0)
                    transpose_queries(2)
                    project_out(at, 0)
                    scores2(2)
                    transpose_probs(at, 1)
                    transpose_queries(3)
                    project_out(at, 1)
                    scores2(3)
                    values2(1)
                    transpose_probs(at, 2)
                    project_out(at, 2)
                    project_out(at, 3)
                    values2(2)
                    transpose_probs(at, 3)
                    project_out(at, 4)
                    project_out(at, 5)
                    values2(3)
                    project_out(at, 6)
                    project_out(at, 7)

                at = Place(3, half).at
                layernorm_tiles(at, A3_LN, 0)
                evacuated(pe, at, A3_LN + NT - 2)
                evacuated(pe, at, A3_LN + NT - 1)
                pieces_split(at, 8)
                for q in range(CHUNKS):
                    tokens = slice(q * 256, (q + 1) * 256)
                    for m in range(4):
                        to = acc_bank(at, A3_UP + 7 * q + m)
                        for f in range(2):
                            for k in range(KC):
                                w = slice(m * 1024 + k * 256 + f * P, m * 1024 + k * 256 + (f + 1) * P)
                                ins = split_mm(to[:, f * 256:(f + 1) * 256], w_hi[:, w], w_lo[:, w],
                                               xn_hi[:, k, tokens], xn_lo[:, k, tokens], k == 0, k == KC - 1)
                        ins.then_inc(acc_rdy.sem, 1)
                    for t in range(2):
                        to = acc_bank(at, A3_LAT + 7 * q + t)
                        token = slice((2 * q + t) * P, (2 * q + t + 1) * P)
                        for k in range(KC):
                            ins = split_mm(to[:, 0:LAT + NE], xn_hi[:, k, token], xn_lo[:, k, token],
                                           f1g_hi[:, k, :], f1g_lo[:, k, :], k == 0, k == KC - 1)
                        ins.then_inc(acc_rdy.sem, 1)
                    evacuated(pe, at, A3_LAT + 7 * q)
                    evacuated(pe, at, A3_LAT + 7 * q + 1)
                    to = acc_bank(at, A3_LATT + 7 * q)
                    for l in range(2):
                        for t in range(2):
                            ins = nc.tensor.transpose(to[:, l * 256 + t * P:l * 256 + (t + 1) * P],
                                                      latn[:, t, l * P:(l + 1) * P], ident[:])
                    ins.then_inc(acc_rdy.sem, 1)
                    for t in range(2):
                        i = 2 * q + t
                        pe.wait_ge(y_free.sem, at(y_free, i - 1))
                        pe.wait_ge(ht_hi_done.sem, at(ht_hi_done, 4 * q + 4))
                        pe.wait_ge(ht_lo_done.sem, at(ht_lo_done, 4 * q + 4))
                        for f in range(INNER // P):
                            w = slice(f * D, (f + 1) * D)
                            split_mm(y[t][:], ht_hi[:, f, t * P:(t + 1) * P], ht_lo[:, f, t * P:(t + 1) * P],
                                     dn_hi[:, w], dn_lo[:, w], f == 0, False)
                        evacuated(pe, at, A3_LATT + 7 * q)
                        for l in range(2):
                            ins = split_mm(y[t][:], latt_hi[:, l, t * P:(t + 1) * P], latt_lo[:, l, t * P:(t + 1) * P],
                                           w23_hi[:, l, :], w23_lo[:, l, :], False, l == 1)
                        ins.then_inc(y_rdy.sem, 1)

        @block.scalar
        def _(act):
            def split_piece(at, stage_no, n):
                act.wait_ge(w_ld[n % 2].sem, at(w_ld[n % 2], n // 2 + 1))
                if stage_no == 1:
                    if n < 4:
                        act.wait_ge(acc_rdy.sem, at(acc_rdy, 0))
                    else:
                        act.wait_ge(y_rdy.sem, at(y_rdy, 0))
                elif stage_no == 2:
                    if n < 2:
                        act.wait_ge(acc_rdy.sem, at(acc_rdy, A2_KV + 4 - ACC2))
                    elif n < 4:
                        act.wait_ge(acc_rdy.sem, at(acc_rdy, A2_QP[-1] + 1 - ACC2))
                    else:
                        act.wait_ge(y_rdy.sem, at(y_rdy, 0))
                elif n < 4:
                    act.wait_ge(acc_rdy.sem, at(acc_rdy, A2_KV + 4 - ACC2))
                else:
                    act.wait_ge(y_rdy.sem, at(y_rdy, 0))
                target, width = piece_target(stage_no, n, 0)
                nc.scalar.copy(target, stage[:, n % 2, 0:width]).then_inc(w_hi_done.sem, 1)

            def transposed_hi(at, n, target, done):
                act.wait_ge(acc_rdy.sem, at(acc_rdy, n + 1))
                nc.scalar.copy(target, blocks(acc[n % 2])).then_inc(done.sem, 1)

            def exps(at, u):
                act.wait_ge(s_sub.sem, at(s_sub, u + 1))
                nc.scalar.activation(prob[:, u % PRING, :], prob[:, u % PRING, :], ACT.Exp).then_inc(s_exp.sem, 1)

            def evacuate_probs(at, u):
                act.wait_ge(pt_rdy.sem, at(pt_rdy, u + 1))
                nc.scalar.copy(probt[:, u % 2, :], pt[:]).then_inc(pt_done.sem, 1)

            def output_hi(i):
                nc.scalar.copy(by_head(ot_hi[:, i % 2, :]), by_sequence(ot[i % 2][:])).then_inc(ot_hi_done.sem, 1)

            act.wait_ge(const_ld.sem, 16 * 9)
            nc.scalar.copy(f1g_hi[:], f1g_raw).then_inc(f1g_hi_done.sem, 1)
            for l in range(2):
                act.wait_ge(w23_rdy.sem, l + 1)
                nc.scalar.copy(w23_hi[:, l, :], y[l][:]).then_inc(w23_hi_done.sem, 1)
            act.wait_ge(f1g_lo_done.sem, 1)
            act.wait_ge(wqk_made.sem, 1)

            with act.Fori(0, HALVES) as half:
                at = Place(1, half).at
                for i in range(NT):
                    transposed_hi(at, A1_CTX + i, tile_of(cx_hi, i), ctx_hi_done)
                split_piece(at, 1, 0)
                split_piece(at, 1, 1)
                for i in range(NT):
                    transposed_hi(at, A1_LN1 + i, tile_of(xn_hi, i), ln_hi_done)
                split_piece(at, 1, 2)
                split_piece(at, 1, 3)
                for m in range(NT // 2):
                    n = A1_KV + m
                    act.wait_ge(acc_rdy.sem, at(acc_rdy, n + 1))
                    kv = acc[n % 2][:].rearrange("p (t c) -> p t c", t=2)
                    nc.scalar.copy(kraw[:, 2 * m:2 * m + 2, :], kv[:, :, 0:P])
                    nc.scalar.copy(vraw[:, 2 * m:2 * m + 2, :], kv[:, :, P:2 * P]).then_inc(acc_free[n % 2].sem, 1)
                for s in range(2):
                    for r in range(REP):
                        n = A1_Q + s * REP + r
                        act.wait_ge(acc_rdy.sem, at(acc_rdy, n + 1))
                        nc.scalar.mul(q1t[:, s * 8:(s + 1) * 8, r, :],
                                      acc[n % 2][:].rearrange("p (b q) -> p b q", b=8), HD1 ** -0.5
                                      ).then_inc(acc_free[n % 2].sem, 1)
                for m in range(2):
                    n = A1_KT + m
                    act.wait_ge(acc_rdy.sem, at(acc_rdy, n + 1))
                    nc.scalar.copy(kt[:, m * COLS:(m + 1) * COLS], acc[n % 2][:]).then_inc(acc_free[n % 2].sem, 1)
                split_piece(at, 1, 4)
                split_piece(at, 1, 5)

                def spread_values(b):
                    if b == 0:
                        act.wait_ge(zone_clear.sem, at(zone_clear, 1))
                        evacuated(act, at, A1_KV + 2)
                        evacuated(act, at, A1_KV + 3)
                    if b >= 2:
                        act.wait_ge(pv_done.sem, at(pv_done, 2 * b - 2))
                    rows = slice((b % 2) * SEQ, (b % 2 + 1) * SEQ)
                    values = vraw[rows, b // 2, :].rearrange("p (i g d) -> p g i d", i=4, g=2)
                    for g2 in range(2):
                        ins = nc.scalar.copy(own_block(b % 2, g2), values[:, g2])
                    ins.then_inc(vbd_done.sem, 1)

                spread_values(0)
                spread_values(1)
                exps(at, 0)
                for u in range(UNITS1 + 1):
                    if u + 1 < UNITS1:
                        exps(at, u + 1)
                    if u < UNITS1:
                        evacuate_probs(at, u)
                    if u >= 4 and u % 4 == 0:
                        i = (u - 4) // 4
                        act.wait_ge(pv_done.sem, at(pv_done, 4 * i + 4))
                        output_hi(i)
                    if u % 2 == 1 and 2 <= (u + 1) // 2 < NSEQ:
                        spread_values((u + 1) // 2)
                for i in range(NT):
                    transposed_hi(at, A1_LN2 + i, tile_of(xn_hi, i), ln_hi_done)

                with act.Fori(0, NG) as turn:
                    at = Place(2, half, turn).at

                    def evacuate_queries(i):
                        n = A2_QP[i]
                        act.wait_ge(acc_rdy.sem, at(acc_rdy, n + 1))
                        nc.scalar.copy(qraw[:, i % 4], blocks(acc[n % 2]))
                        for h in range(REP):
                            ins = nc.scalar.activation(squares[:, n % 2, h, :], acc[n % 2][:, h * P:(h + 1) * P],
                                                       ACT.Square,
                                                       accum_out=qss[:, (i // 2) % 2, i % 2, h:h + 1])
                        ins.then_inc(acc_free[n % 2].sem, 1)

                    def evacuate_transposed_queries(c):
                        for t in range(2):
                            n = A2_QT[2 * c + t]
                            act.wait_ge(acc_rdy.sem, at(acc_rdy, n + 1))
                            nc.scalar.copy(q2t[:, c % 2, t],
                                           acc[n % 2][:].rearrange("p (h b q) -> p b h q", h=REP, b=2)
                                           ).then_inc(acc_free[n % 2].sem, 1)

                    def outputs_hi(c):
                        for i in (2 * c, 2 * c + 1):
                            act.wait_ge(ot_rdy.sem, at(ot_rdy, i + 1))
                            output_hi(i)

                    for n in range(4):
                        split_piece(at, 2, n)
                    for m in range(NT // 2):
                        n = A2_KV + m
                        act.wait_ge(acc_rdy.sem, at(acc_rdy, n + 1))
                        kv = acc[n % 2][:].rearrange("p (t c) -> p t c", t=2)
                        nc.scalar.copy(kraw[:, 2 * m:2 * m + 2, :], kv[:, :, 0:P])
                        for t in range(2):
                            ins = nc.scalar.activation(squares[:, n % 2, t, :], kv[:, t, 0:P], ACT.Square,
                                                       accum_out=kss[:, 2 * m + t:2 * m + t + 1])
                        ins.then_inc(kv_act.sem, 1)
                        if m % 2 == 1:
                            split_piece(at, 2, 4 + m // 2)
                    for i in range(4):
                        evacuate_queries(i)
                    for m in range(2):
                        n = A2_KT + m
                        act.wait_ge(acc_rdy.sem, at(acc_rdy, n + 1))
                        nc.scalar.mul(kt[:, m * COLS:(m + 1) * COLS], acc[n % 2][:], qkn[:, 2:3]
                                      ).then_inc(acc_free[n % 2].sem, 1)
                    evacuate_transposed_queries(0)
                    evacuate_queries(4)
                    evacuate_queries(5)
                    exps(at, 0)
                    evacuate_transposed_queries(1)
                    evacuate_queries(6)
                    evacuate_probs(at, 0)
                    evacuate_queries(7)
                    exps(at, 1)
                    outputs_hi(0)
                    evacuate_transposed_queries(2)
                    evacuate_probs(at, 1)
                    evacuate_transposed_queries(3)
                    exps(at, 2)
                    outputs_hi(1)
                    evacuate_probs(at, 2)
                    exps(at, 3)
                    outputs_hi(2)
                    evacuate_probs(at, 3)
                    outputs_hi(3)

                at = Place(3, half).at
                for n in range(4):
                    split_piece(at, 3, n)
                for i in range(NT):
                    transposed_hi(at, A3_LN + i, tile_of(xn_hi, i), ln_hi_done)
                for n in range(4, 8):
                    split_piece(at, 3, n)
                for q in range(CHUNKS):
                    def rectify(m):
                        n = A3_UP + 7 * q + m
                        act.wait_ge(acc_rdy.sem, at(acc_rdy, n + 1))
                        nc.scalar.activation(relu[:, m % 2, :], acc[n % 2][:], ACT.Relu
                                             ).then_inc(acc_free[n % 2].sem, 1)

                    def hidden_hi(m):
                        act.wait_ge(hsq_done.sem, at(hsq_done, 4 * q + m + 1))
                        nc.scalar.copy(ht_hi[:, 2 * m:2 * m + 2, :].rearrange("p f t -> p (f t)"), hsq[:, m % 2, :]
                                       ).then_inc(ht_hi_done.sem, 1)

                    rectify(0)
                    rectify(1)
                    hidden_hi(0)
                    rectify(2)
                    hidden_hi(1)
                    rectify(3)
                    hidden_hi(2)
                    hidden_hi(3)
                    n = A3_LATT + 7 * q
                    act.wait_ge(acc_rdy.sem, at(acc_rdy, n + 1))
                    nc.scalar.copy(latt_hi[:].rearrange("p l t -> p (l t)"), acc[n % 2][:]).then_inc(latt_hi_done.sem, 1)

        @block.vector
        def _(dve):
            def rest(target, whole, high):
                return nc.vector.tensor_tensor(target, whole, high.bitcast(F32), ALU.subtract)

            def transposed_lo(at, n, hi, lo, done, k):
                dve.wait_ge(done.sem, at(done, k))
                rest(lo, blocks(acc[n % 2]), hi).then_inc(acc_free[n % 2].sem, 1)

            def statistics(at, first, i):
                nc.vector.bn_stats(bn[:, i, :], x[:, i, :]).then_inc(ln_bn.sem, 1)
                dve.wait_ge(ln_bn.sem, at(ln_bn, first + i + 1))
                carry_wait_dve()
                nc.vector.bn_aggr(mv[:, i, :], bn[:, i, :]).then_inc(ln_aggr.sem, 1)
                dve.wait_ge(ln_aggr.sem, at(ln_aggr, first + i + 1))
                nc.vector.tensor_scalar(veps[:, i:i + 1], mv[:, i, 1:2], EPS, None, ALU.add).then_inc(ln_veps.sem, 1)

            def normalise(at, first, base, i):
                dve.wait_ge(ln_rstd.sem, at(ln_rstd, first + i + 1))
                if i >= 2:
                    dve.wait_ge(acc_rdy.sem, at(acc_rdy, base + i - 1))
                nc.vector.tensor_scalar(xn[:, i % 2, :], x[:, i, :], mv[:, i, 0:1], rstd[:, i:i + 1],
                                        ALU.subtract, ALU.mult).then_inc(ln_xn.sem, 1)

            def layernorm(at, first, base, before=lambda i: None):
                for i in range(NT + 1):
                    if i < NT:
                        normalise(at, first, base, i)
                    if i >= 1:
                        transposed_lo(at, base + i - 1, tile_of(xn_hi, i - 1), tile_of(xn_lo, i - 1),
                                      ln_hi_done, first + i)
                    before(i + 2)

            def add_and_max(at, u, added):
                dve.wait_ge(sc_rdy.sem, at(sc_rdy, u + 1))
                grouped = prob[:, u % PRING, :].rearrange("p (g k) -> p g k", g=8)
                nc.vector.tensor_tensor(grouped, sc[:].rearrange("p (g k) -> p g k", g=8),
                                        added[:].unsqueeze(1).to_broadcast([P, 8, SEQ]), ALU.add).then_inc(s_add.sem, 1)
                dve.wait_ge(s_add.sem, at(s_add, u + 1))
                nc.vector.tensor_reduce(pmax[:, u % PRING, :], grouped, AX_X, ALU.max).then_inc(s_max.sem, 1)

            def sums(at, u):
                dve.wait_ge(s_exp.sem, at(s_exp, u + 1))
                nc.vector.tensor_reduce(psum_[:, u % PRING, :],
                                        prob[:, u % PRING, :].rearrange("p (g k) -> p g k", g=8),
                                        AX_X, ALU.add).then_inc(s_sum.sem, 1)
                dve.wait_ge(s_sum.sem, at(s_sum, u + 1))
                nc.vector.reciprocal(prec[:, u % PRING, :], psum_[:, u % PRING, :]).then_inc(s_rec.sem, 1)

            def output_lo(at, i):
                dve.wait_ge(ot_hi_done.sem, at(ot_hi_done, i + 1))
                rest(by_head(ot_lo[:, i % 2, :]), by_sequence(ot[i % 2][:]), by_head(ot_hi[:, i % 2, :])).then_inc(ot_lo_done.sem, 1)

            def update_x(at, i):
                dve.wait_ge(y_rdy.sem, at(y_rdy, i + 1))
                nc.vector.tensor_tensor(x[:, i, :], y[i % 2][:], x[:, i, :], ALU.add).then_inc(y_free.sem, 1)

            dve.wait_ge(const_ld.sem, 16 * 9)
            dve.wait_ge(const_made.sem, 1)
            nc.vector.tensor_scalar(qkn[:, 2:3], qkn[:, 0:1], qkn[:, 1:2], HD2 ** -0.5, ALU.mult, ALU.mult
                                    ).then_inc(wqk_made.sem, 1)
            for l in range(2):
                dve.wait_ge(w23_hi_done.sem, l + 1)
                rest(w23_lo[:, l, :], y[l][:], w23_hi[:, l, :]).then_inc(w23_lo_done.sem, 1)

            with dve.Fori(0, HALVES) as half:
                at = Place(1, half).at
                for i in range(NT):
                    transposed_lo(at, A1_CTX + i, tile_of(cx_hi, i), tile_of(cx_lo, i), ctx_hi_done, i + 1)
                    dve.wait_ge(x_ld[i // 2].sem, at(x_ld[i // 2], 1))
                    statistics(at, 0, i)
                layernorm(at, 0, A1_LN1)

                def spread_keys(b):
                    if b == 0:
                        evacuated(dve, at, A1_KT)
                        evacuated(dve, at, A1_KT + 1)
                    if b >= 2:
                        dve.wait_ge(sc_rdy.sem, at(sc_rdy, 2 * b - 2))
                    nc.vector.tensor_tensor(kbd[:, b % 2], kt[:, b * SEQ:(b + 1) * SEQ].unsqueeze(1).to_broadcast(
                        [P, NG, SEQ]), spread(gsel[:], NG, SEQ), ALU.mult).then_inc(kbd_done.sem, 1)

                spread_keys(0)
                spread_keys(1)
                for v in range(UNITS1 + 6):
                    if v % 2 == 0 and 2 <= v // 2 + 1 < NSEQ:
                        spread_keys(v // 2 + 1)
                    if v < UNITS1:
                        add_and_max(at, v, causal)
                    if 1 <= v <= UNITS1:
                        sums(at, v - 1)
                    if v >= 6 and v % 4 == 2 and (v - 6) // 4 < NT:
                        output_lo(at, (v - 6) // 4)
                    if v >= 9 and v % 4 == 1:
                        i = (v - 9) // 4
                        update_x(at, i)
                        dve.wait_ge(y_free.sem, at(y_free, i + 1))
                        statistics(at, NT, i)
                layernorm(at, NT, A1_LN2)

                with dve.Fori(0, NG) as turn:
                    at = Place(2, half, turn).at

                    def query_variance(c):
                        evacuated(dve, at, A2_QP[2 * c])
                        evacuated(dve, at, A2_QP[2 * c + 1])
                        nc.vector.tensor_scalar(qve[:, c % 2, :], qss[:, c % 2].rearrange("p t h -> p (t h)"),
                                                1.0 / HD2, EPS, ALU.mult, ALU.add).then_inc(q_ve.sem, 1)

                    def scale_queries(c):
                        dve.wait_ge(q_rs.sem, at(q_rs, c + 1))
                        t = 2 * (c % 2)
                        q = qraw[:, t:t + 2].rearrange("p t h d -> p (t h) d")
                        nc.vector.tensor_tensor(q, q, spread(qrs[:, c % 2, :], 2 * REP, HD2), ALU.mult
                                                ).then_inc(q_nrm.sem, 1)

                    def outputs_lo(c):
                        output_lo(at, 2 * c)
                        output_lo(at, 2 * c + 1)

                    def updates_x(c):
                        update_x(at, 2 * c)
                        update_x(at, 2 * c + 1)

                    for m in range(NT // 2):
                        n = A2_KV + m
                        dve.wait_ge(kv_act.sem, at(kv_act, m + 1))
                        if m == 0:
                            dve.wait_ge(zone_clear.sem, 2 * half + 2)
                        for b in range(2):
                            rows = slice(b * SEQ, (b + 1) * SEQ)
                            ins = nc.vector.tensor_copy(
                                vpad[rows, 2 * m:2 * m + 2, b, :],
                                acc[n % 2][rows, :].rearrange("p (t c) -> p t c", t=2)[:, :, P:2 * P])
                        ins.then_inc(acc_free[n % 2].sem, 1)
                    nc.vector.tensor_scalar(kve[:], kss[:], 1.0 / HD2, EPS, ALU.mult, ALU.add).then_inc(k_ve.sem, 1)
                    query_variance(0)
                    dve.wait_ge(k_rs.sem, at(k_rs, 1))
                    nc.vector.tensor_tensor(kraw[:], kraw[:], spread(krs[:], NT, HD2), ALU.mult).then_inc(k_nrm.sem, 1)
                    scale_queries(0)
                    query_variance(1)
                    scale_queries(1)
                    add_and_max(at, 0, mask)
                    sums(at, 0)
                    query_variance(2)
                    add_and_max(at, 1, mask)
                    scale_queries(2)
                    sums(at, 1)
                    outputs_lo(0)
                    query_variance(3)
                    scale_queries(3)
                    add_and_max(at, 2, mask)
                    update_x(at, 0)
                    sums(at, 2)
                    add_and_max(at, 3, mask)
                    update_x(at, 1)
                    outputs_lo(1)
                    sums(at, 3)
                    updates_x(1)
                    outputs_lo(2)
                    updates_x(2)
                    outputs_lo(3)
                    updates_x(3)

                at = Place(3, half).at
                dve.wait_ge(y_free.sem, at(y_free, 0))
                statistics(at, 0, 0)
                statistics(at, 0, 1)
                layernorm(at, 0, A3_LN, lambda i: statistics(at, 0, i) if i < NT else None)
                for q in range(CHUNKS):
                    def square(m):
                        evacuated(dve, at, A3_UP + 7 * q + m)
                        if 4 * q + m >= 2:
                            dve.wait_ge(ht_lo_done.sem, at(ht_lo_done, 4 * q + m - 1))
                        nc.vector.tensor_tensor(hsq[:, m % 2, :], relu[:, m % 2, :], relu[:, m % 2, :], ALU.mult
                                                ).then_inc(hsq_done.sem, 1)

                    def hidden_lo(m):
                        dve.wait_ge(ht_hi_done.sem, at(ht_hi_done, 4 * q + m + 1))
                        rest(ht_lo[:, 2 * m:2 * m + 2, :].rearrange("p f t -> p (f t)"), hsq[:, m % 2, :],
                             ht_hi[:, 2 * m:2 * m + 2, :].rearrange("p f t -> p (f t)")).then_inc(ht_lo_done.sem, 1)

                    square(0)
                    square(1)
                    hidden_lo(0)
                    square(2)
                    hidden_lo(1)
                    square(3)
                    hidden_lo(2)
                    hidden_lo(3)
                    for t in range(2):
                        n = A3_LAT + 7 * q + t
                        i = 2 * q + t
                        dve.wait_ge(acc_rdy.sem, at(acc_rdy, n + 1))
                        carry_wait_dve()
                        nc.vector.max(top8[:, t, :], acc[n % 2][:, LAT:LAT + NE]).then_inc(top_done.sem, 1)
                        dve.wait_ge(top_done.sem, at(top_done, i + 1))
                        nc.vector.tensor_tensor(route[:, t:t + 1], top8[:, t, 0:1], top8[:, t, 1:2], ALU.add
                                                ).then_inc(route_done.sem, 1)
                        dve.wait_ge(route_done.sem, at(route_done, i + 1))
                        nc.vector.tensor_scalar(latn[:, t, :], acc[n % 2][:, 0:LAT], route[:, t:t + 1], None, ALU.mult
                                                ).then_inc(acc_free[n % 2].sem, 1)
                    n = A3_LATT + 7 * q
                    dve.wait_ge(latt_hi_done.sem, at(latt_hi_done, q + 1))
                    rest(latt_lo[:].rearrange("p l t -> p (l t)"), acc[n % 2][:],
                         latt_hi[:].rearrange("p l t -> p (l t)")).then_inc(acc_free[n % 2].sem, 1)
                    for t in range(2):
                        i = 2 * q + t
                        dve.wait_ge(y_rdy.sem, at(y_rdy, i + 1))
                        nc.vector.bn_stats(ybn[:, t, :], y[t][:]).then_inc(y_bn.sem, 1)
                        dve.wait_ge(y_bn.sem, at(y_bn, i + 1))
                        carry_wait_dve()
                        nc.vector.bn_aggr(ymv[:, t, :], ybn[:, t, :]).then_inc(y_aggr.sem, 1)
                        dve.wait_ge(y_aggr.sem, at(y_aggr, i + 1))
                        nc.vector.tensor_scalar(yve[:, t:t + 1], ymv[:, t, 1:2], EPS, None, ALU.add
                                                ).then_inc(y_ve.sem, 1)
                        if i >= 2:
                            dve.wait_ge(x_out.sem, at(x_out, i - 1))
                        nc.vector.scalar_tensor_tensor(znorm[:, t, :], y[t][:], ymv[:, t, 0:1], gamma[:],
                                                       ALU.subtract, ALU.mult).then_inc(y_free.sem, 1)
                        dve.wait_ge(y_free.sem, at(y_free, i + 1))
                        dve.wait_ge(y_rs.sem, at(y_rs, i + 1))
                        dve.wait_ge(xb_done.sem, at(xb_done, i + 1))
                        nc.vector.scalar_tensor_tensor(x[:, i, :], znorm[:, t, :], yrs[:, t:t + 1], x[:, i, :],
                                                       ALU.mult, ALU.add).then_inc(x_out.sem, 1)

        @block.gpsimd
        def _(pool):
            def split_piece(at, stage_no, n):
                pool.wait_ge(w_hi_done.sem, at(w_hi_done, n + 1))
                high, width = piece_target(stage_no, n, 0)
                low, _ = piece_target(stage_no, n, 1)
                nc.gpsimd.tensor_tensor(low, stage[:, n % 2, 0:width], high.bitcast(F32), ALU.subtract
                                        ).then_inc(w_lo_done.sem, 1)

            def rsqrt(target, source, width):
                return nc.gpsimd.tensor_tensor(target, source, mhalf[:, 0:width], ALU.pow)

            def layernorm_rstd(at, first, i):
                pool.wait_ge(ln_veps.sem, at(ln_veps, first + i + 1))
                rsqrt(rstd[:, i:i + 1], veps[:, i:i + 1], 1).then_inc(ln_rstd.sem, 1)

            def subtract_max(at, u):
                pool.wait_ge(s_max.sem, at(s_max, u + 1))
                pr = prob[:, u % PRING, :].rearrange("p (g k) -> p g k", g=8)
                nc.gpsimd.tensor_tensor(pr, pr, spread(pmax[:, u % PRING, :], 8, SEQ), ALU.subtract
                                        ).then_inc(s_sub.sem, 1)

            def normalise_probs(at, u):
                pool.wait_ge(s_rec.sem, at(s_rec, u + 1))
                pr = prob[:, u % PRING, :].rearrange("p (g k) -> p g k", g=8)
                nc.gpsimd.tensor_tensor(pr, pr, spread(prec[:, u % PRING, :], 8, SEQ), ALU.mult).then_inc(s_nrm.sem, 1)

            steps = [0]

            def made(ins):
                steps[0] += 1
                ins.then_inc(const_step.sem, 1)
                pool.wait_ge(const_step.sem, steps[0])

            made(nc.gpsimd.memset(ident[:], 0.0))
            made(nc.gpsimd.affine_select(out=ident[:], in_=ident[:], compare_op=ALU.not_equal, fill=1.0, base=0,
                                         pattern=[[-1, P]], channel_multiplier=1))
            made(nc.gpsimd.memset(causal[:], 0.0))
            for b in range(2):
                part = causal[b * SEQ:(b + 1) * SEQ, :]
                made(nc.gpsimd.affine_select(out=part, in_=part, compare_op=ALU.is_ge, fill=-1e30, base=0,
                                             pattern=[[-1, SEQ]], channel_multiplier=1))
            made(nc.gpsimd.memset(gsel[:], 1.0))
            made(nc.gpsimd.affine_select(out=gsel[:], in_=gsel[:], compare_op=ALU.is_ge, fill=0.0, base=0,
                                         pattern=[[-HD1, NG]], channel_multiplier=1))
            made(nc.gpsimd.affine_select(out=gsel[:], in_=gsel[:], compare_op=ALU.is_ge, fill=0.0, base=HD1 - 1,
                                         pattern=[[HD1, NG]], channel_multiplier=-1))
            made(nc.gpsimd.memset(scrap[:, 1:2], 0.0))
            nc.gpsimd.memset(mhalf[:], -0.5).then_inc(const_made.sem, 1)
            pool.wait_ge(const_made.sem, 1)
            pool.wait_ge(const_ld.sem, 16 * 9)
            pool.wait_ge(f1g_hi_done.sem, 1)
            nc.gpsimd.tensor_tensor(f1g_lo[:], f1g_raw, f1g_hi[:].bitcast(F32), ALU.subtract).then_inc(f1g_lo_done.sem, 1)

            with pool.Fori(0, HALVES) as half:
                at = Place(1, half).at
                pool.wait_ge(y_rdy.sem, at(y_rdy, 0))
                carry_wait_pool()
                nc.gpsimd.memset(zone[:, 0:1024], 0.0).then_inc(zone_clear.sem, 1)
                for i in range(NT):
                    layernorm_rstd(at, 0, i)
                for n in range(6):
                    split_piece(at, 1, n)
                for v in range(UNITS1 + 1):
                    if v < UNITS1:
                        subtract_max(at, v)
                    if v >= 1:
                        normalise_probs(at, v - 1)
                for i in range(NT):
                    layernorm_rstd(at, NT, i)
                pool.wait_ge(pv_done.sem, at(pv_done, UNITS1))
                carry_wait_pool()
                nc.gpsimd.memset(zone[:], 0.0).then_inc(zone_clear.sem, 1)

                with pool.Fori(0, NG) as turn:
                    at = Place(2, half, turn).at

                    def query_rsqrt(c):
                        pool.wait_ge(q_ve.sem, at(q_ve, c + 1))
                        rsqrt(qrs[:, c % 2, :], qve[:, c % 2, :], 2 * REP).then_inc(q_rs.sem, 1)

                    for n in range(5):
                        split_piece(at, 2, n)
                    pool.wait_ge(k_ve.sem, at(k_ve, 1))
                    rsqrt(krs[:], kve[:], NT).then_inc(k_rs.sem, 1)
                    split_piece(at, 2, 5)
                    query_rsqrt(0)
                    query_rsqrt(1)
                    subtract_max(at, 0)
                    normalise_probs(at, 0)
                    query_rsqrt(2)
                    subtract_max(at, 1)
                    normalise_probs(at, 1)
                    query_rsqrt(3)
                    subtract_max(at, 2)
                    normalise_probs(at, 2)
                    subtract_max(at, 3)
                    normalise_probs(at, 3)

                at = Place(3, half).at
                for n in range(4):
                    split_piece(at, 3, n)
                for i in range(NT):
                    layernorm_rstd(at, 0, i)
                for n in range(4, 8):
                    split_piece(at, 3, n)
                for i in range(NT):
                    pool.wait_ge(ln_xn.sem, at(ln_xn, i + 1))
                    nc.gpsimd.tensor_tensor(x[:, i, :], x[:, i, :], beta[:], ALU.add).then_inc(xb_done.sem, 1)
                for i in range(NT):
                    pool.wait_ge(y_ve.sem, at(y_ve, i + 1))
                    rsqrt(yrs[:, i % 2:i % 2 + 1], yve[:, i % 2:i % 2 + 1], 1).then_inc(y_rs.sem, 1)


def kernel(**inputs):
    from concourse import bacc
    from concourse.bass_utils import run_bass_kernel_spmd

    a = {k: np.asarray(v) for k, v in inputs.items()}

    def by_partition(w):
        return w.reshape(-1, P, w.shape[-1]).transpose(1, 0, 2)

    def flat(w):
        return w.reshape(P, -1)

    wq = by_partition(a["L0_attn_wq"]).reshape(P, KC, NG, REP, HD1).transpose(0, 1, 3, 2, 4)
    wkv = np.concatenate([by_partition(a["L0_attn_wk"]), by_partition(a["L0_attn_wv"])], axis=2)
    wo = a["L0_attn_wo"].reshape(NG, REP, HD1, D).transpose(0, 2, 1, 3)
    w_self = np.concatenate([flat(wkv), flat(wq), flat(wo)], axis=1)
    cross = []
    for g in range(NG):
        kv = slice(g * HD2, (g + 1) * HD2)
        qs = slice(g * REP * HD2, (g + 1) * REP * HD2)
        ck = by_partition(a["L0_xattn_Wk"][kv].T)
        cv = by_partition(a["L0_xattn_Wv"][kv].T)
        cq = by_partition(a["L0_xattn_Wq"][qs].T)
        co = by_partition(a["L0_xattn_Wo"][:, qs].T)
        cross.append(np.concatenate([flat(np.concatenate([ck, cv], axis=2)), flat(cq), flat(co)], axis=1))
    w_cross = np.stack(cross)
    down = by_partition(a["L0_ffn_down_w"]).reshape(P, 4, 1024).transpose(1, 0, 2)
    up = by_partition(a["L0_ffn_up_w"]).reshape(P, KC, 4, 256).transpose(2, 0, 1, 3).reshape(4, P, 1024)
    w_ffn = np.concatenate([down, up])
    f1g = np.concatenate([by_partition(a["L0_ffn_fc1_w"]), by_partition(a["L0_ffn_gate_w"])], axis=2)
    arrays = {
        "x": a["x"].reshape(HALVES, NT, P, D),
        "ctx": a["ctx_4096"].reshape(HALVES, NT, P, D),
        "mask": a["mask_1x1xSxS2_ff0"].reshape(SEQ, SEQ),
        "w_self": w_self,
        "w_cross": w_cross,
        "q_norm": a["L0_xattn_q_norm_w"].reshape(P, 1),
        "k_norm": a["L0_xattn_k_norm_w"].reshape(P, 1),
        "w_ffn": w_ffn,
        "f1g": f1g,
        "expert_t": by_partition(a["L0_ffn_expert_w"].T),
        "fc2": by_partition(a["L0_ffn_fc2_w"]),
        "gamma": a["L0_ffn_ln_gamma"].reshape(1, D),
        "beta": a["L0_ffn_ln_beta"].reshape(1, D),
    }
    arrays = {f"in_{k}": np.ascontiguousarray(v) for k, v in arrays.items()}
    nc = bacc.Bacc("TRN2", target_bir_lowering=False, num_devices=1, dynamic_dma_scratch_size=1024)
    args = [nc.dram_tensor(k, v.shape, mybir.dt.from_np(v.dtype), kind="ExternalInput").ap() for k, v in arrays.items()]
    out = nc.dram_tensor("out_x", (HALVES, NT, P, D), F32, kind="ExternalOutput").ap()
    decoder_block(nc, *args, out)
    result = run_bass_kernel_spmd(nc, [arrays], core_ids=[0])
    return result.results[0]["out_x"].reshape(BATCH, SEQ, D)
```
